# Optimizing a Trainium2 kernel written in Bass

```python
import numpy as np
import jax
import jax.numpy as jnp

def _softmax(x, axis=-1):
    return jax.nn.softmax(x, axis=axis)

def _gelu(x):
    return jax.nn.gelu(x, approximate=True)

def _silu(x):
    return jax.nn.silu(x)

def _sigmoid(x):
    return jax.nn.sigmoid(x)

def _layernorm(x, axis=-1, eps=1e-05):
    m = jnp.mean(x, axis=axis, keepdims=True)
    v = jnp.var(x, axis=axis, keepdims=True)
    return (x - m) / jnp.sqrt(v + eps)

def _scatter_add(tgt, idx, src, axis=0):
    return tgt.at[idx].add(src)

def _segment_sum(src, seg, n):
    return jax.ops.segment_sum(src, seg, n)
kernel_name = 'mk_flamingo_gated_d1_seqx_r2_a7821a'

def setup_inputs(seed: int=0):
    np.random.seed(seed)
    _w = jnp.asarray

    def _rec_inputs():
        import jax
        import jax.numpy as jnp
        _rk = jax.random.key(seed)
        x = -0.0003929 + 0.9999 * jax.random.normal(jax.random.fold_in(_rk, 1), (16, 100, 512), jnp.float32)
        _lenS = 100 - jax.random.randint(jax.random.fold_in(_rk, 7), (16,), 0, max(1, 100 // 4) + 1, jnp.int32)
        _lenS2 = 722 - jax.random.randint(jax.random.fold_in(_rk, 8), (16,), 0, max(1, 722 // 4) + 1, jnp.int32)
        _ctx_1024P = jax.random.normal(jax.random.fold_in(_rk, 11), (16, 16, 512), jnp.float32)
        _ctx_1024c = jax.random.dirichlet(jax.random.fold_in(_rk, 511), 0.3 * jnp.ones((16,), jnp.float32), (16, 722))
        _ctx_1024t = jnp.einsum('bsk,bkd->bsd', _ctx_1024c, _ctx_1024P)
        _ctx_1024t = _ctx_1024t * jax.lax.rsqrt(jnp.mean(jnp.square(_ctx_1024t)) + 1e-12) * 0.953939
        ctx_1024 = 0.00208318 + 0.999174 * (_ctx_1024t + 0.3 * jax.random.normal(jax.random.fold_in(_rk, 611), (16, 722, 512), jnp.float32))
        _validS = jnp.arange(100)[None, :] < _lenS[:, None]
        _validS2 = jnp.arange(722)[None, :] < _lenS2[:, None]
        _causal = jnp.tril(jnp.ones((100, 100), dtype=bool))
        mask_BxSxS2_ff0 = jnp.where(jnp.ones((16, 100, 722), dtype=bool), 0.0, -1000000000.0).astype(jnp.float32)
        _g = jax.random.normal(jax.random.fold_in(_rk, 9001), (2, 1), jnp.float32)
        _g = jnp.sign(_g) * jnp.maximum(jnp.abs(_g), 1.0) + (_g == 0) * 1.0
        g_xattn = _g[0]
        g_ffn = _g[1]
        return (x, ctx_1024, mask_BxSxS2_ff0, g_xattn, g_ffn)
    x, ctx_1024, mask_BxSxS2_ff0, g_xattn, g_ffn = _rec_inputs()

    def _L0_xattn_setup():
        import jax, jax.numpy as jnp
        import numpy as np
        NUM_HEADS = 16
        DIM = 512
        key = jax.random.key(seed)
        ks = jax.random.split(key, 12)
        B, N, T, C = (4, 2048, 77, DIM)
        s = 1.0 / np.sqrt(C)
        return {'hidden_states': jax.random.normal(ks[0], (B, N, C), jnp.float32), 'encoder_hidden_states': jax.random.normal(ks[1], (B, T, C), jnp.float32), 'attention_mask': jnp.zeros((B, N, T), jnp.float32), 'Wq': jax.random.normal(ks[2], (C, C), jnp.float32) * s, 'bq': jnp.zeros((C,), jnp.float32), 'Wk': jax.random.normal(ks[3], (C, C), jnp.float32) * s, 'bk': jnp.zeros((C,), jnp.float32), 'Wv': jax.random.normal(ks[4], (C, C), jnp.float32) * s, 'bv': jnp.zeros((C,), jnp.float32), 'Wo': jax.random.normal(ks[5], (C, C), jnp.float32) * s, 'bo': jnp.zeros((C,), jnp.float32)}
    _L0_xattn_all = _L0_xattn_setup()
    _L0_xattn_in = {k: v for k, v in _L0_xattn_all.items() if k in ('Wq', 'bq', 'Wk', 'bk', 'Wv', 'bv', 'Wo', 'bo')}
    del _L0_xattn_all

    def _L0_ffn_setup():
        import jax, jax.numpy as jnp
        import numpy as np
        B, S, E, H, NE, TOP_K = (4, 1024, 512, 1024, 8, 2)
        key = jax.random.key(seed)
        ks = jax.random.split(key, 5)
        s = 0.02
        return {'x': jax.random.normal(ks[0], (B, S, E), jnp.float32), 'w1': jax.random.normal(ks[1], (NE, E, H), jnp.float32) * s, 'b1': jnp.zeros((NE, H), jnp.float32), 'w2': jax.random.normal(ks[2], (NE, H, H), jnp.float32) * s, 'b2': jnp.zeros((NE, H), jnp.float32), 'w3': jax.random.normal(ks[3], (NE, H, E), jnp.float32) * s, 'b3': jnp.zeros((NE, E), jnp.float32), 'gate_w': jax.random.normal(ks[4], (E, NE), jnp.float32) * s, 'gate_b': jnp.zeros((NE,), jnp.float32)}
    _L0_ffn_all = _L0_ffn_setup()
    _L0_ffn_in = {k: v for k, v in _L0_ffn_all.items() if k in ('w1', 'b1', 'w2', 'b2', 'w3', 'b3', 'gate_w', 'gate_b')}
    del _L0_ffn_all
    return {'x': x, 'ctx_1024': ctx_1024, 'mask_BxSxS2_ff0': mask_BxSxS2_ff0, 'g_xattn': g_xattn, 'g_ffn': g_ffn, 'L0_xattn_Wq': _L0_xattn_in['Wq'], 'L0_xattn_bq': _L0_xattn_in['bq'], 'L0_xattn_Wk': _L0_xattn_in['Wk'], 'L0_xattn_bk': _L0_xattn_in['bk'], 'L0_xattn_Wv': _L0_xattn_in['Wv'], 'L0_xattn_bv': _L0_xattn_in['bv'], 'L0_xattn_Wo': _L0_xattn_in['Wo'], 'L0_xattn_bo': _L0_xattn_in['bo'], 'L0_ffn_w1': _L0_ffn_in['w1'], 'L0_ffn_b1': _L0_ffn_in['b1'], 'L0_ffn_w2': _L0_ffn_in['w2'], 'L0_ffn_b2': _L0_ffn_in['b2'], 'L0_ffn_w3': _L0_ffn_in['w3'], 'L0_ffn_b3': _L0_ffn_in['b3'], 'L0_ffn_gate_w': _L0_ffn_in['gate_w'], 'L0_ffn_gate_b': _L0_ffn_in['gate_b']}

def reference(x, ctx_1024, mask_BxSxS2_ff0, g_xattn, g_ffn, L0_xattn_Wq, L0_xattn_bq, L0_xattn_Wk, L0_xattn_bk, L0_xattn_Wv, L0_xattn_bv, L0_xattn_Wo, L0_xattn_bo, L0_ffn_w1, L0_ffn_b1, L0_ffn_w2, L0_ffn_b2, L0_ffn_w3, L0_ffn_b3, L0_ffn_gate_w, L0_ffn_gate_b):
    import jax
    import jax.numpy as jnp

    def _L0_xattn_ref(hidden_states, encoder_hidden_states, attention_mask, Wq, bq, Wk, bk, Wv, bv, Wo, bo):
        import jax, jax.numpy as jnp
        import numpy as np
        NUM_HEADS = 16
        DIM = 512
        B, N, C = hidden_states.shape
        T = encoder_hidden_states.shape[1]
        H = NUM_HEADS
        D = C // H
        q = (hidden_states @ Wq.T + bq).reshape(B, N, H, D).transpose(0, 2, 1, 3)
        k = (encoder_hidden_states @ Wk.T + bk).reshape(B, T, H, D).transpose(0, 2, 1, 3)
        v = (encoder_hidden_states @ Wv.T + bv).reshape(B, T, H, D).transpose(0, 2, 1, 3)
        scale = 1.0 / jnp.sqrt(jnp.asarray(D, q.dtype))
        scores = jnp.einsum('bhnd,bhtd->bhnt', q, k) * scale + attention_mask[:, None, :, :]
        attn = jax.nn.softmax(scores, axis=-1)
        out = jnp.einsum('bhnt,bhtd->bhnd', attn, v)
        out = out.transpose(0, 2, 1, 3).reshape(B, N, C)
        return out @ Wo.T + bo

    def _L0_ffn_ref(x, w1, b1, w2, b2, w3, b3, gate_w, gate_b):
        import jax, jax.numpy as jnp
        import numpy as np
        B, S, E, H, NE, TOP_K = (4, 1024, 512, 1024, 8, 2)
        gate_weights = jax.nn.softmax(x @ gate_w + gate_b, axis=-1)
        topk_vals, topk_idx = jax.lax.top_k(gate_weights, TOP_K)
        h = jax.nn.gelu(jnp.einsum('bse,neh->bsnh', x, w1) + b1, approximate=False)
        h = jax.nn.gelu(jnp.einsum('bsnh,nhk->bsnk', h, w2) + b2, approximate=False)
        expert_out = jnp.einsum('bsnh,nhe->bsne', h, w3) + b3
        gathered = jnp.take_along_axis(expert_out, topk_idx[..., None], axis=2)
        return jnp.sum(topk_vals[..., None] * gathered, axis=2)
    x = x + jnp.tanh(g_xattn[0]) * _L0_xattn_ref(_layernorm(x, axis=-1), ctx_1024, mask_BxSxS2_ff0, L0_xattn_Wq, L0_xattn_bq, L0_xattn_Wk, L0_xattn_bk, L0_xattn_Wv, L0_xattn_bv, L0_xattn_Wo, L0_xattn_bo)
    x = x + jnp.tanh(g_ffn[0]) * _L0_ffn_ref(_layernorm(x, axis=-1), L0_ffn_w1, L0_ffn_b1, L0_ffn_w2, L0_ffn_b2, L0_ffn_w3, L0_ffn_b3, L0_ffn_gate_w, L0_ffn_gate_b)
    return x

_drawn_inputs = setup_inputs


def setup_inputs(seed=0):
    import zlib

    import numpy as np

    out = dict(_drawn_inputs(seed))
    spreads = {'L0_xattn_bq': (0.0, 0.547),
     'L0_xattn_bk': (0.0, 0.8),
     'L0_xattn_bv': (0.0, 0.1),
     'L0_xattn_bo': (0.0, 0.1),
     'L0_ffn_b1': (0.0, 0.8),
     'L0_ffn_b2': (0.0, 0.8),
     'L0_ffn_b3': (0.0, 0.322),
     'L0_ffn_gate_b': (0.0, 0.585)}
    factors = {'L0_ffn_w1': 4.34, 'L0_ffn_w2': 4.071, 'L0_ffn_w3': 3.441}
    for name, (base, spread) in spreads.items():
        noise = np.random.default_rng([zlib.crc32(name.encode()), seed]).standard_normal(out[name].shape)
        drawn = base * np.exp(spread * noise) if base else spread * noise
        out[name] = jnp.asarray(drawn.astype(out[name].dtype))
    for name, factor in factors.items():
        out[name] = (out[name] * factor).astype(out[name].dtype)
    return out
```

```python
from contextlib import ExitStack

import numpy as np

import concourse.bass as bass
from concourse import mybir

F32 = mybir.dt.float32
F32R = mybir.dt.float32r
I32 = mybir.dt.int32
U32 = mybir.dt.uint32
ALU = mybir.AluOpType
ACT = mybir.ActivationFunctionType
AX = mybir.AxisListType

P = 128
B, S, D = 16, 100, 512
T = 722
H, HD = 16, 32
DT = D // P
HQ = P // HD
HP = H // 2
NT = 6
TT = 121
TP = NT * TT
HALF = T // 2
EVEN = HALF + HALF % 2
HALVES = [(0, EVEN), (EVEN, EVEN)]
SCALE = float(HD) ** -0.5
EPS = 1e-5
E, HID = 8, 1024
HT = HID // P
BLOCK = 256
NBLOCKS = (2 * B * S + E * (BLOCK - 1)) // BLOCK
REGION = B * S + BLOCK
SPARE_ROW = E * REGION
ROWS = SPARE_ROW + BLOCK
ROW = D + 2
MAXB = -(-B * S // BLOCK)
TPB = BLOCK // P
BIG = float(np.finfo(np.float32).max)

PRODUCTS = ((0, 0), (0, 1), (1, 0))
SCORE_BUFS = 3
LN_STEPS = 6
PADS = 5
ROUTE_CONSTS = 12
STEP_EITHER = 11
ROUTE_STEPS = STEP_EITHER + 10
HELD_AFTER = (5, 6)
EARLIER, IN_ALL = 64, 128


def build(nc, x, ctx_in, mask, g_x, g_f, wq, bq, wk, bk, wv, bv, wo, bo,
          w1, b1, w2, b2, w3, b3, gw, gb, out):
    xs_dram = nc.dram_tensor("expert_in_rows", [ROWS, ROW], F32, kind="Internal").ap()

    top = ExitStack()
    with top:
        def sb(stack, name, shape, dt=F32):
            return stack.enter_context(nc.sbuf_tensor(name, shape, dt))

        def sem(name):
            return top.enter_context(nc.semaphore(name))

        bank_rows = top.enter_context(nc.psum_tensor("bank_rows", [P, 8, 512], F32))
        banks = [bank_rows[:, i, :] for i in range(8)]

        ident = sb(top, "ident", [P, P])
        filling = sb(top, "filling", [P, TPB, ROW])
        expert_end = sb(top, "expert_end", [1, E], I32)
        block_expert = sb(top, "block_expert", [1, NBLOCKS], I32)
        block_row = sb(top, "block_row", [1, NBLOCKS], I32)

        attention(nc, sb, sem, bank_rows, banks, ident, filling, expert_end, block_expert, block_row,
                  xs_dram, x, ctx_in, mask, g_x, g_f, wq, bq, wk, bk, wv, bv, wo, bo, gw, gb, out)
        experts(nc, sb, sem, banks, ident, filling, expert_end, block_expert, block_row,
                xs_dram, w1, b1, w2, b2, w3, b3, out)


def batch_rows(a, n):
    return a[n] if isinstance(n, int) else a[bass.ds(n, 1), :, :].rearrange("a s d -> (a s) d")


def out_rows(out, n):
    return out[n * S:(n + 1) * S, :] if isinstance(n, int) else out[bass.ds(n * S, S), :]


def attention(nc, sb, sem, bank_rows, banks, ident, filling, expert_end, block_expert, block_row,
              xs_dram, x, ctx_in, mask, g_x, g_f, wq, bq, wk, bk, wv, bv, wo, bo, gw, gb, out):
    score_bank, pt_bank, o_bank = banks[0:4], banks[4:6], banks[6:8]
    score_pair = [bank_rows[0:S, 2 * k:2 * k + 2, :] for k in range(2)]

    bk_loaded = sem("bk_loaded")
    small_loaded = sem("small_loaded")
    gates_loaded = sem("gates_loaded")
    raw_loaded = [sem("wk_loaded"), sem("wv_loaded")]
    wq_wo_loaded = sem("wq_wo_loaded")
    w_hi = sem("w_hi")
    w_lo = sem("w_lo")
    ident_step = sem("ident_step")
    pads_zero = sem("pads_zero")
    gates_ready = sem("gates_ready")
    fill_step = sem("fill_step")
    spare_filled = sem("spare_filled")
    route_consts = sem("route_consts")
    ctx_loaded = sem("ctx_loaded")
    mask_loaded = sem("mask_loaded")
    xln_loaded = sem("xln_loaded")
    xres_loaded = sem("xres_loaded")
    ctx_transposed = sem("ctx_transposed")
    ctx_hi = sem("ctx_hi")
    ctx_lo = sem("ctx_lo")
    k_ready = sem("k_ready")
    k_hi = sem("k_hi")
    k_lo = sem("k_lo")
    v_ready = sem("v_ready")
    v_hi = sem("v_hi")
    v_lo = sem("v_lo")
    ln_step = [sem("ln1_step"), sem("ln2_step")]
    ln_log = [sem("ln1_log"), sem("ln2_log")]
    xn_ready = sem("xn_ready")
    xn_transposed = sem("xn_transposed")
    xt_copied = sem("xt_copied")
    q_ready = sem("q_ready")
    q_scaled = sem("q_scaled")
    q_hi = sem("q_hi")
    q_lo = sem("q_lo")
    q_again = sem("q_again")
    scores_ready = sem("scores_ready")
    scored = sem("scored")
    waits_carried = sem("waits_carried")
    turn_wait_carried = sem("turn_wait_carried")
    probs_ready = sem("probs_ready")
    pt_ready = sem("pt_ready")
    pt_hi = sem("pt_hi")
    pt_lo = sem("pt_lo")
    pair_done = sem("pair_done")
    pair_part = sem("pair_part")
    pair_kept = sem("pair_kept")
    o_turned = sem("o_turned")
    o_part = sem("o_part")
    o_step = sem("o_step")
    o_transposed = sem("o_transposed")
    ot_copied = sem("ot_copied")
    y_ready = sem("y_ready")
    x1_step = sem("x1_step")
    x2_ready = sem("x2_ready")
    x2_transposed = sem("x2_transposed")
    x2t_copied = sem("x2t_copied")
    logits_ready = sem("logits_ready")
    route_step = sem("route_step")
    route_exp = sem("route_exp")
    counted = sem("pairs_counted")
    x2_copied = sem("x2_copied")
    x1_stored = sem("x1_stored")
    scatter_go = sem("scatter_go")
    rows_scattered = sem("rows_scattered")
    table_step = sem("table_step")

    mem = ExitStack()
    with mem:
        wq_sb = sb(mem, "wq_sb", [P, DT, D])
        wo_sb = sb(mem, "wo_sb", [P, DT, D])
        wk_hl = [sb(mem, f"wk_{n}", [P, DT, D], F32R) for n in ("high", "low")]
        wv_hl = [sb(mem, f"wv_{n}", [P, DT, D], F32R) for n in ("high", "low")]
        gw_sb = sb(mem, "gw_sb", [P, DT, E])
        gb_sb = sb(mem, "gb_sb", [S, E])
        bq_sb = sb(mem, "bq_sb", [P, DT])
        bk_sb = sb(mem, "bk_sb", [P, DT])
        bv_sb = sb(mem, "bv_sb", [S, D])
        bo_sb = sb(mem, "bo_sb", [S, D])
        gates_raw = sb(mem, "gates_raw", [P, 2])
        gate_x = sb(mem, "gate_x", [P, 1])
        eps = sb(mem, "eps", [P, 1])
        gate_f = sb(mem, "gate_f", [P, 1])
        ctx_sb = sb(mem, "ctx_sb", [TT, NT, D])
        ctx_t = [sb(mem, f"ctx_t_{n}", [P, DT, TP], F32R) for n in ("high", "low")]
        k_t = sb(mem, "k_t", [P, DT, 2, 2 * EVEN], F32R)
        v_sb = sb(mem, "v_sb", [TT, NT, H, 2, HD], F32R)
        q_pad = [sb(mem, f"q_pad_{n}", [P, DT, HQ, S], F32R) for n in ("high", "low")]
        x_ln = sb(mem, "x_ln", [S, D])
        x_res = sb(mem, "x_res", [S, D])
        xn = sb(mem, "xn", [S, D])
        x2 = sb(mem, "x2", [S, 2, ROW])
        xt = sb(mem, "xt", [P, DT, S])
        x2t = sb(mem, "x2t", [P, DT, S])
        q_sb = sb(mem, "q_sb", [P, 2, DT, S])
        mask_sb = sb(mem, "mask_sb", [S, T])
        probs = sb(mem, "probs", [S, SCORE_BUFS, TP])
        p_t = sb(mem, "p_t", [TT, 2, NT, 2, S], F32R)
        pair_low = sb(mem, "pair_low", [2 * HD, 2, S])
        o_heads = sb(mem, "o_heads", [2 * HD, H, S])
        neg_max = sb(mem, "neg_max", [S, H])
        exp_sum = sb(mem, "exp_sum", [S, H])
        recip_sum = sb(mem, "recip_sum", [S, H])
        o_sb = sb(mem, "o_sb", [S, 2, D])
        o_t = sb(mem, "o_t", [P, DT, S])
        stats = sb(mem, "stats", [S, 2, 6])
        moments = sb(mem, "moments", [S, 2, 2])
        rstd = sb(mem, "rstd", [S, 2, 6])

        before = sb(mem, "before", [S, S])
        ones = sb(mem, "ones", [S, P])
        expert_id = sb(mem, "expert_id", [S, E])
        first_row = sb(mem, "first_row", [P, E])
        next_row = sb(mem, "next_row", [P, E])
        token = sb(mem, "token", [S, 1])
        logits = sb(mem, "logits", [S, E])
        row_max = sb(mem, "row_max", [S, 1])
        shifted = sb(mem, "shifted", [S, E])
        row_sum = sb(mem, "row_sum", [S, 2])
        gates = sb(mem, "gates", [S, 2, E])
        top_gate = sb(mem, "top_gate", [S, 8])
        top_id = sb(mem, "top_id", [S, 8], U32)
        top_idf = sb(mem, "top_idf", [S, 2])
        chosen = sb(mem, "chosen", [S, 2, E])
        either = sb(mem, "either", [S, E])
        row_of = sb(mem, "row_of", [S, E])
        row_pick = sb(mem, "row_pick", [S, 2, E])
        row_f = sb(mem, "row_f", [S, 2])
        pair_row = sb(mem, "pair_row", [S, 2], U32)
        block_rows_below = sb(mem, "block_rows_below", [1, E, MAXB])
        block_id = sb(mem, "block_id", [1, NBLOCKS, E])
        block_start = sb(mem, "block_start", [1, NBLOCKS])
        pairs_of = sb(mem, "pairs_of", [1, E])
        over = sb(mem, "over", [1, E, MAXB])
        blocks_of = sb(mem, "blocks_of", [1, E])
        blocks_end = sb(mem, "blocks_end", [1, E])
        up_to = sb(mem, "up_to", [1, E, E])
        blocks_to = sb(mem, "blocks_to", [1, E, E])
        shift = sb(mem, "shift", [1, E])
        ended = sb(mem, "ended", [1, 2, NBLOCKS, E])
        table_f = sb(mem, "table_f", [1, 3, NBLOCKS])
        block = mem.enter_context(nc.Block())

        @block.gpsimd
        def _(pool):
            pads = (ctx_sb[96:TT, NT - 1, :], eps[:], q_pad[0][:].bitcast(F32), q_pad[1][:].bitcast(F32),
                    probs[:, :, T:TP])
            for k, (pad, value) in enumerate(zip(pads, (0.0, EPS, 0.0, 0.0, 0.0))):
                nc.gpsimd.memset(pad, value).then_inc(pads_zero, 1)
                pool.wait_ge(pads_zero, k + 1)
            nc.gpsimd.memset(ident[:], 0.0).then_inc(ident_step, 1)
            pool.wait_ge(ident_step, 1)
            nc.gpsimd.affine_select(out=ident[:], in_=ident[:], compare_op=ALU.not_equal, fill=1.0,
                                    base=0, pattern=[[-1, P]], channel_multiplier=1).then_inc(ident_step, 1)
            nc.gpsimd.memset(filling[:], 0.0).then_inc(fill_step, 1)
            pool.wait_ge(fill_step, 1)
            for t in range(TPB):
                nc.gpsimd.iota(filling[:, t, D:D + 1].bitcast(I32), [[0, 1]], base=B * S + t * P,
                               channel_multiplier=1).then_inc(fill_step, 1)
                pool.wait_ge(fill_step, t + 2)
            made = 0
            for dst, pattern, step in ((expert_id, [[1, E]], 0), (first_row, [[REGION, E]], 0),
                                       (next_row, [[REGION, E]], 0), (token, [[0, 1]], 1),
                                       (block_rows_below, [[0, E], [BLOCK, MAXB]], 0),
                                       (block_id, [[1, NBLOCKS], [0, E]], 0), (block_start, [[BLOCK, NBLOCKS]], 0)):
                nc.gpsimd.iota(dst[:], pattern, base=0, channel_multiplier=step,
                               allow_small_or_imprecise_dtypes=True).then_inc(route_consts, 1)
                made += 1
                pool.wait_ge(route_consts, made)
            for dst, value in ((before, 0.0), (ones, 1.0), (up_to, 1.0)):
                nc.gpsimd.memset(dst[:], value).then_inc(route_consts, 1)
                made += 1
                pool.wait_ge(route_consts, made)
            nc.gpsimd.affine_select(out=before[:], in_=before[:], compare_op=ALU.is_ge, fill=1.0,
                                    base=0, pattern=[[-1, S]], channel_multiplier=1).then_inc(route_consts, 1)
            made += 1
            pool.wait_ge(route_consts, made)
            nc.gpsimd.affine_select(out=up_to[:], in_=up_to[:], compare_op=ALU.is_ge, fill=0.0,
                                    base=0, pattern=[[1, E], [-1, E]], channel_multiplier=0).then_inc(route_consts, 1)
            assert made + 1 == ROUTE_CONSTS

            def scatter(b):
                pool.wait_ge(route_step, ROUTE_STEPS * b + ROUTE_STEPS)
                pool.wait_ge(x2_copied, b + 1)
                pool.sem_inc(scatter_go, 1)
                for k in range(2):
                    nc.gpsimd.indirect_dma_start(
                        out=xs_dram, out_offset=bass.IndirectOffsetOnAxis(ap=pair_row[:, k:k + 1], axis=0),
                        in_=x2[:, k, :], in_offset=None).then_inc(rows_scattered, 16)

            with pool.Fori(0, B) as b:
                scatter(b)
            pool.wait_ge(rows_scattered, 32 * B)

        @block.sync
        def _(sp):
            def load_ctx(n):
                src = batch_rows(ctx_in, n)
                for i in range(NT):
                    rows = min(TT, T - i * TT)
                    sp.dma_start(ctx_sb[0:rows, i, :], src[i * TT:i * TT + rows, :]).then_inc(ctx_loaded, 16)

            def spread(src, rows):
                return src.rearrange("(a n) -> a n", a=1).broadcast_to([rows, src.shape[0]])

            sp.dma_start(x_ln[:], x[0]).then_inc(xln_loaded, 16)
            sp.dma_start(wo_sb[:], wk.rearrange("(t p) n -> p t n", p=P)).then_inc(raw_loaded[0], 16)
            sp.dma_start(gates_raw[:, 0:1], spread(g_x, P)).then_inc(gates_loaded, 16)
            sp.dma_start(gates_raw[:, 1:2], spread(g_f, P)).then_inc(gates_loaded, 16)
            sp.dma_start(bk_sb[:], bk).then_inc(bk_loaded, 16)
            sp.wait_ge(pads_zero, 1)
            load_ctx(0)
            sp.dma_start(wq_sb[:], wv.rearrange("(t p) n -> p t n", p=P)).then_inc(raw_loaded[1], 16)
            sp.dma_start(bq_sb[:], bq).then_inc(small_loaded, 16)
            sp.dma_start(gw_sb[:], gw.rearrange("(t p) n -> p t n", p=P)).then_inc(small_loaded, 16)
            sp.dma_start(gb_sb[:], spread(gb, S)).then_inc(small_loaded, 16)
            sp.dma_start(bv_sb[:], spread(bv, S)).then_inc(small_loaded, 16)
            sp.dma_start(bo_sb[:], spread(bo, S)).then_inc(small_loaded, 16)
            sp.wait_ge(w_lo, 2)
            sp.dma_start(wq_sb[:], wq.rearrange("(t p) n -> p t n", p=P)).then_inc(wq_wo_loaded, 16)
            sp.dma_start(wo_sb[:], wo.rearrange("(t p) n -> p t n", p=P)).then_inc(wq_wo_loaded, 16)
            sp.dma_start(mask_sb[:], mask[0]).then_inc(mask_loaded, 16)
            sp.dma_start(x_res[:], x[0]).then_inc(xres_loaded, 16)
            sp.wait_ge(fill_step, TPB + 1)
            sp.dma_start(xs_dram[SPARE_ROW:ROWS, :].rearrange("(t p) d -> p t d", p=P),
                         filling[:]).then_inc(spare_filled, 16)
            sp.dma_start(out[B * S:, :].rearrange("(t p) d -> p t d", p=P),
                         filling[:, :, 0:D]).then_inc(spare_filled, 16)

            def store(b):
                sp.wait_ge(x1_step, 2 * b + 2)
                sp.dma_start(out_rows(out, b), x_res[:]).then_inc(x1_stored, 16)
                sp.wait_ge(x2_ready, b + 1)
                sp.wait_ge(x1_stored, 16 * b + 16)

            with sp.Fori(0, B - 1) as b:
                sp.wait_ge(ctx_transposed, NT * b + NT)
                load_ctx(b + 1)
                sp.wait_ge(xn_ready, b + 1)
                sp.dma_start(x_ln[:], batch_rows(x, b + 1)).then_inc(xln_loaded, 16)
                sp.wait_ge(scored, H * b + H)
                sp.dma_start(mask_sb[:], batch_rows(mask, b + 1)).then_inc(mask_loaded, 16)
                store(b)
                sp.dma_start(x_res[:], batch_rows(x, b + 1)).then_inc(xres_loaded, 16)
            store(B - 1)
            sp.wait_ge(spare_filled, 32)

        @block.tensor
        def _(pe):
            def transpose_ctx(n, i):
                if i == 0:
                    pe.wait_ge(ctx_loaded, 16 * NT * n + 16 * NT)
                    pe.wait_ge(scored, H * n)
                if i == len(score_bank):
                    pe.wait_ge(pt_lo, 2 * H * n)
                for m in range(DT):
                    last = nc.tensor.transpose(banks[i][:, m * TT:(m + 1) * TT],
                                               ctx_sb[:, i, m * P:(m + 1) * P], ident[0:TT, 0:TT])
                last.then_inc(ctx_transposed, 1)

            def keys(n, half, m):
                j = half * DT + m
                if half == 0:
                    pe.wait_ge(ctx_lo, NT * n + max(3, m + 1))
                else:
                    pe.wait_ge(ctx_lo, NT * n + NT)
                    pe.wait_ge(k_lo, 4 * DT * n + 2 * m + 2)
                off, size = HALVES[half]
                steps = [(c, a, b) for c in range(DT) for a, b in PRODUCTS]
                for s, (c, a, b) in enumerate(steps):
                    last = nc.tensor.matmul(score_bank[m][:, 0:size], wk_hl[a][:, c, m * P:(m + 1) * P],
                                            ctx_t[b][:, c, off:off + size],
                                            start=(s == 0), stop=(s == len(steps) - 1))
                last.then_inc(k_ready, 1)

            def values(n, i):
                if i < 4:
                    pe.wait_ge(k_lo, 4 * DT * n + 2 * (DT + i + 1))
                elif i == 4:
                    pe.wait_ge(xt_copied, n + 1)
                else:
                    pe.wait_ge(q_scaled, 2 * n + 1)
                steps = [(c, a, b) for c in range(DT) for a, b in PRODUCTS]
                for s, (c, a, b) in enumerate(steps):
                    last = nc.tensor.matmul(banks[i][0:TT, :], ctx_t[a][:, c, i * TT:(i + 1) * TT],
                                            wv_hl[b][:, c, :], start=(s == 0), stop=(s == len(steps) - 1))
                last.then_inc(v_ready, 1)

            def transpose_xn(n):
                pe.wait_ge(xn_ready, n + 1)
                pe.wait_ge(ctx_lo, NT * n + 5)
                for m in range(DT):
                    last = nc.tensor.transpose(pt_bank[0][:, m * S:(m + 1) * S],
                                               xn[:, m * P:(m + 1) * P], ident[0:S, 0:S])
                last.then_inc(xn_transposed, 1)

            def queries(n):
                pe.wait_ge(xt_copied, n + 1)
                pe.wait_ge(ctx_lo, NT * n + NT)
                for m in range(DT):
                    for c in range(DT):
                        last = nc.tensor.matmul(pt_bank[1][:, m * S:(m + 1) * S], wq_sb[:, c, m * P:(m + 1) * P],
                                                xt[:, c, :], start=(c == 0), stop=(c == DT - 1))
                last.then_inc(q_ready, 1)

            def scores(b, h):
                m, q = divmod(h, HQ)
                if h >= 2:
                    pe.wait_ge(scored, H * b + h - 1)
                for half in range(2):
                    off = half * HALF
                    for a in range(2):
                        last = nc.tensor.matmul(score_pair[h % 2][:, half, 0:EVEN], q_pad[a][:, m, q, :],
                                                k_t[:, m, q // 2, off:off + EVEN], start=(a == 0), stop=(a == 1))
                last.then_inc(scores_ready, 1)

            def transpose_probs(b, h):
                pe.wait_ge(probs_ready, H * b + h + 1)
                for g in range(2):
                    if h > 0:
                        pe.wait_ge(pt_lo, 2 * H * b + 2 * (h - 1) + g + 1)
                    for i in range(3):
                        t0 = (3 * g + i) * TT
                        last = nc.tensor.transpose(pt_bank[g][0:TT, i * S:(i + 1) * S],
                                                   probs[:, h % SCORE_BUFS, t0:t0 + TT], ident[0:S, 0:S])
                    last.then_inc(pt_ready, 1)

            def attend(b, h):
                pair = h // 2
                pe.wait_ge(pt_lo, 2 * H * b + 2 * h + 2)
                if h == 2:
                    pe.wait_ge(route_step, ROUTE_STEPS * b)
                if h % 2 == 0 and pair >= 2:
                    pe.wait_ge(pair_kept, HP * b + pair - 1)
                for i in range(NT):
                    last = nc.tensor.matmul(o_bank[pair % 2][0:2 * HD, (h % 2) * 2 * S:(h % 2 + 1) * 2 * S],
                                            v_sb[:, i, h, :, :], p_t[:, h % 2, i, :, :],
                                            start=(i == 0), stop=(i == NT - 1))
                if h % 2 == 1:
                    last.then_inc(pair_done, 1)

            def turn_o(b):
                pe.wait_ge(pair_kept, HP * b + HP)
                pe.sem_inc(turn_wait_carried, 1)
                for h in range(H):
                    last = nc.tensor.transpose(o_bank[h // 8][0:S, (h % 8) * 2 * HD:(h % 8 + 1) * 2 * HD],
                                               o_heads[:, h, :], ident[0:2 * HD, 0:2 * HD])
                    if h % 8 == 7:
                        last.then_inc(o_turned, 1)

            def heads(b, n):
                for s in range(1, H + 3):
                    if s == 1:
                        pe.wait_ge(v_lo, NT * b + 4)
                    if s < H:
                        scores(b, s)
                    if s == 2:
                        pe.wait_ge(v_lo, NT * b + NT)
                    if 2 <= s < H + 2:
                        transpose_probs(b, s - 2)
                    if s >= 3:
                        attend(b, s - 3)
                    if n is not None and s >= H:
                        transpose_ctx(n, 2 * (s - H))
                        transpose_ctx(n, 2 * (s - H) + 1)

            def transpose_o(b):
                pe.wait_ge(o_step, 5 * b + 5)
                for m in range(DT):
                    last = nc.tensor.transpose(o_bank[0][:, m * S:(m + 1) * S],
                                               o_sb[:, 1, m * P:(m + 1) * P], ident[0:S, 0:S])
                last.then_inc(o_transposed, 1)

            def project_o(b):
                pe.wait_ge(ot_copied, b + 1)
                for c in range(DT):
                    last = nc.tensor.matmul(o_bank[1][0:S, :], o_t[:, c, :], wo_sb[:, c, :],
                                            start=(c == 0), stop=(c == DT - 1))
                last.then_inc(y_ready, 1)

            def transpose_x2(b):
                pe.wait_ge(x2_ready, b + 1)
                for m in range(DT):
                    last = nc.tensor.transpose(o_bank[0][:, m * S:(m + 1) * S],
                                               x2[:, 0, m * P:(m + 1) * P], ident[0:S, 0:S])
                last.then_inc(x2_transposed, 1)

            def router_logits(b):
                pe.wait_ge(x2t_copied, b + 1)
                for c in range(DT):
                    last = nc.tensor.matmul(o_bank[1][0:S, 0:E], x2t[:, c, :], gw_sb[:, c, :],
                                            start=(c == 0), stop=(c == DT - 1))
                last.then_inc(logits_ready, 1)

            def count_pairs(b):
                pe.wait_ge(route_step, ROUTE_STEPS * b + STEP_EITHER)
                nc.tensor.matmul(o_bank[1][0:S, EARLIER:EARLIER + E], before[:], either[:], start=True, stop=True)
                nc.tensor.matmul(o_bank[1][:, IN_ALL:IN_ALL + E], ones[:], either[:],
                                 start=True, stop=True).then_inc(counted, 1)

            def between(b, n):
                if b is None:
                    pe.wait_ge(w_lo, 1)
                if n is not None:
                    keys(n, 0, 0)
                if b is not None:
                    turn_o(b)
                if n is not None:
                    for m in range(1, DT):
                        keys(n, 0, m)
                if b is not None:
                    transpose_o(b)
                if n is not None:
                    keys(n, 1, 0)
                    keys(n, 1, 1)
                if b is not None:
                    project_o(b)
                if n is not None:
                    keys(n, 1, 2)
                    keys(n, 1, 3)
                    transpose_xn(n)
                    if b is None:
                        pe.wait_ge(w_lo, 2)
                    values(n, 0)
                if b is not None:
                    transpose_x2(b)
                if n is not None:
                    values(n, 1)
                    if b is None:
                        pe.wait_ge(wq_wo_loaded, 32)
                        pe.wait_ge(small_loaded, 16 * 5)
                        pe.wait_ge(route_consts, ROUTE_CONSTS)
                if b is not None:
                    router_logits(b)
                if n is not None:
                    queries(n)
                    values(n, 2)
                    values(n, 3)
                if b is not None:
                    count_pairs(b)
                if n is not None:
                    pe.wait_ge(q_again, HQ * n + HQ)
                    pe.wait_ge(q_lo, HQ * n + HQ)
                    pe.wait_ge(v_lo, NT * n + 2)
                    scores(n, 0)
                    values(n, 4)
                    values(n, 5)

            pe.wait_ge(ident_step, 2)
            pe.wait_ge(pads_zero, PADS)
            for i in range(NT):
                transpose_ctx(0, i)
            between(None, 0)
            with pe.Fori(0, B - 1) as b:
                heads(b, b + 1)
                between(b, b + 1)
            heads(B - 1, None)
            between(B - 1, None)

        @block.scalar
        def _(act):
            def ctx_high(n, i):
                act.wait_ge(ctx_transposed, NT * n + i + 1)
                src = banks[i][:, 0:DT * TT].rearrange("p (m t) -> p m t", m=DT)
                nc.scalar.activation(ctx_t[0][:, :, i * TT:(i + 1) * TT], src, ACT.Copy).then_inc(ctx_hi, 1)

            def rstd_start(which, n):
                act.wait_ge(ln_step[which], LN_STEPS * n + 2)
                nc.scalar.activation(rstd[:, which, 0:1], moments[:, which, 1:2], ACT.Ln,
                                     bias=eps[0:S, 0:1]).then_inc(ln_log[which], 1)
                act.wait_ge(ln_log[which], 2 * n + 1)
                nc.scalar.activation(rstd[:, which, 1:2], rstd[:, which, 0:1], ACT.Exp,
                                     scale=-0.5).then_inc(ln_log[which], 1)

            def keys_high(n, j):
                half, m = divmod(j, DT)
                off, size = HALVES[half]
                act.wait_ge(k_ready, 2 * DT * n + j + 1)
                for pair, rows in enumerate((slice(0, P // 2), slice(P // 2, P))):
                    nc.scalar.activation(k_t[rows, m, pair, off:off + size], score_bank[m][rows, 0:size], ACT.Identity,
                                         bias=bk_sb[rows, m:m + 1]).then_inc(k_hi, 1)

            def values_high(n, i):
                act.wait_ge(v_ready, NT * n + i + 1)
                nc.scalar.activation(v_sb[:, i, :, 0, :],
                                     banks[i][0:TT, :].rearrange("t (h d) -> t h d", h=H),
                                     ACT.Copy).then_inc(v_hi, 1)

            def queries_high(n):
                act.wait_ge(q_scaled, 2 * n + 2)
                for q in range(HQ):
                    rows = slice(q * HD, (q + 1) * HD)
                    again = slice((q + 2) % HQ * HD, ((q + 2) % HQ + 1) * HD)
                    nc.scalar.activation(q_pad[0][rows, :, q, :], q_sb[rows, 1, :, :], ACT.Copy).then_inc(q_hi, 1)
                    nc.scalar.activation(q_pad[0][again, :, q, :], q_sb[rows, 1, :, :], ACT.Copy).then_inc(q_again, 1)

            def pair_low_part(b, pair):
                act.wait_ge(pair_done, HP * b + pair + 1)
                act.wait_ge(pair_kept, HP * b + pair)
                src = o_bank[pair % 2][0:2 * HD, 0:4 * S].rearrange("p (a x s) -> p a x s", a=2, x=2)
                nc.scalar.activation(pair_low[:], src[:, :, 1, :], ACT.Copy).then_inc(pair_part, 1)

            def exps(b, h):
                act.wait_ge(scored, H * b + h + 1)
                p = probs[:, h % SCORE_BUFS, 0:T]
                nc.scalar.activation(p, p, ACT.Exp, bias=neg_max[:, h:h + 1], scale=-1.0,
                                     accum_out=exp_sum[:, h:h + 1]).then_inc(probs_ready, 1)

            def probs_high(b, h):
                for g in range(2):
                    act.wait_ge(pt_ready, 2 * H * b + 2 * h + g + 1)
                    nc.scalar.activation(p_t[:, h % 2, 3 * g:3 * g + 3, 0, :],
                                         pt_bank[g][0:TT, 0:3 * S].rearrange("t (i s) -> t i s", i=3),
                                         ACT.Copy).then_inc(pt_hi, 1)

            def heads(b, n):
                for s in range(2, H + 4):
                    if s == 2:
                        probs_high(b, 0)
                    if s <= H:
                        exps(b, s - 1)
                    if 2 < s < H + 2:
                        probs_high(b, s - 2)
                    if s >= 5 and s % 2 == 1:
                        pair_low_part(b, (s - 5) // 2)
                    if n is not None and s >= H:
                        ctx_high(n, s - H)

            def o_low_parts(b):
                for g in range(2):
                    act.wait_ge(o_turned, 2 * b + g + 1)
                    src = o_bank[g][0:S, :].rearrange("s (h x d) -> s h x d", h=8, x=2)[:, :, 1, :]
                    nc.scalar.activation(o_sb[:, 0, g * 256:(g + 1) * 256].rearrange("s (h d) -> s h d", h=8),
                                         src, ACT.Copy).then_inc(o_part, 1)

            def copy_transposed(src_bank, dst, ready, ready_at, done):
                act.wait_ge(ready, ready_at)
                nc.scalar.activation(dst[:], src_bank[:, 0:DT * S].rearrange("p (m s) -> p m s", m=DT),
                                     ACT.Copy).then_inc(done, 1)

            def between(b, n):
                if n is not None:
                    for i in range(0 if b is None else 4, NT):
                        ctx_high(n, i)
                    rstd_start(0, n)
                if b is None:
                    weights_high(1)
                if b is not None:
                    o_low_parts(b)
                if n is not None:
                    for j in range(4):
                        keys_high(n, j)
                if b is not None:
                    copy_transposed(o_bank[0], o_t, o_transposed, b + 1, ot_copied)
                if n is not None:
                    for j in range(4, 8):
                        keys_high(n, j)
                if b is not None:
                    rstd_start(1, b)
                if n is not None:
                    copy_transposed(pt_bank[0], xt, xn_transposed, n + 1, xt_copied)
                    values_high(n, 0)
                if b is not None:
                    copy_transposed(o_bank[0], x2t, x2_transposed, b + 1, x2t_copied)
                    act.wait_ge(rows_scattered, 32 * b)
                    nc.scalar.activation(x2[:, 1, 0:D], x2[:, 0, 0:D], ACT.Copy).then_inc(x2_copied, 1)
                if n is not None:
                    values_high(n, 1)
                if b is not None:
                    act.wait_ge(route_step, ROUTE_STEPS * b + 3)
                    nc.scalar.activation(gates[:, 0, :], shifted[:], ACT.Exp,
                                         accum_out=row_sum[:, 0:1]).then_inc(route_exp, 1)
                if n is not None:
                    queries_high(n)
                    for i in range(2, NT):
                        if i == NT - 1:
                            exps(n, 0)
                        values_high(n, i)

            def weights_high(k):
                act.wait_ge(raw_loaded[k], 16)
                nc.scalar.activation((wk_hl, wv_hl)[k][0][:], (wo_sb, wq_sb)[k][:], ACT.Copy).then_inc(w_hi, 1)

            weights_high(0)
            act.wait_ge(gates_loaded, 32)
            nc.scalar.activation(gate_x[:], gates_raw[:, 0:1], ACT.Tanh).then_inc(gates_ready, 1)
            nc.scalar.activation(gate_f[:], gates_raw[:, 1:2], ACT.Tanh).then_inc(gates_ready, 1)
            act.wait_ge(pads_zero, PADS)
            act.wait_ge(bk_loaded, 16)
            nc.scalar.preload_act_table_set("natural_log_exp_and_others")
            between(None, 0)
            with act.Fori(0, B - 1) as b:
                heads(b, b + 1)
                between(b, b + 1)
            heads(B - 1, None)
            between(B - 1, None)

        @block.vector
        def _(dve):
            def held():
                dve.sem_inc(waits_carried, 1)

            def ln_stats(which, n, src):
                nc.vector.bn_stats(stats[:, which, :], src).then_inc(ln_step[which], 1)
                dve.wait_ge(ln_step[which], LN_STEPS * n + 1)
                held()
                nc.vector.bn_aggr(moments[:, which, :], stats[:, which, :]).then_inc(ln_step[which], 1)
                dve.wait_ge(ln_step[which], LN_STEPS * n + 2)
                nc.vector.tensor_scalar_add(rstd[:, which, 2:3], moments[:, which, 1:2], EPS).then_inc(ln_step[which], 1)

            def ln_apply(which, n, src, dst, done):
                r = rstd[:, which, :]
                dve.wait_ge(ln_log[which], 2 * n + 2)
                dve.wait_ge(ln_step[which], LN_STEPS * n + 3)
                nc.vector.scalar_tensor_tensor(r[:, 3:4], r[:, 1:2], r[:, 1:2], r[:, 2:3],
                                               ALU.mult, ALU.mult).then_inc(ln_step[which], 1)
                dve.wait_ge(ln_step[which], LN_STEPS * n + 4)
                nc.vector.tensor_scalar(r[:, 4:5], r[:, 3:4], -0.5, 1.5, ALU.mult, ALU.add).then_inc(ln_step[which], 1)
                dve.wait_ge(ln_step[which], LN_STEPS * n + 5)
                nc.vector.tensor_tensor(r[:, 5:6], r[:, 4:5], r[:, 1:2], ALU.mult).then_inc(ln_step[which], 1)
                dve.wait_ge(ln_step[which], LN_STEPS * n + 6)
                nc.vector.tensor_scalar(dst, src, moments[:, which, 0:1], r[:, 5:6],
                                        ALU.subtract, ALU.mult).then_inc(done, 1)

            def ctx_low(n, i):
                dve.wait_ge(ctx_hi, NT * n + i + 1)
                src = banks[i][:, 0:DT * TT].rearrange("p (m t) -> p m t", m=DT)
                at = slice(i * TT, (i + 1) * TT)
                nc.vector.tensor_tensor(ctx_t[1][:, :, at], src, ctx_t[0][:, :, at].bitcast(F32),
                                        ALU.subtract).then_inc(ctx_lo, 1)

            def keys_low(n, j):
                half, m = divmod(j, DT)
                off, size = HALVES[half]
                for pair, rows in enumerate((slice(0, P // 2), slice(P // 2, P))):
                    others = slice(P // 2, P) if pair == 0 else slice(0, P // 2)
                    dve.wait_ge(k_hi, 2 * (2 * DT * n + j) + pair + 1)
                    nc.vector.scalar_tensor_tensor(k_t[others, m, pair, off:off + size], score_bank[m][rows, 0:size],
                                                   bk_sb[rows, m:m + 1], k_t[rows, m, pair, off:off + size].bitcast(F32),
                                                   ALU.add, ALU.subtract).then_inc(k_lo, 1)

            def values_low(n, i):
                dve.wait_ge(v_hi, NT * n + i + 1)
                nc.vector.tensor_tensor(v_sb[:, i, :, 1, :],
                                        banks[i][0:TT, :].rearrange("t (h d) -> t h d", h=H),
                                        v_sb[:, i, :, 0, :].bitcast(F32), ALU.subtract).then_inc(v_lo, 1)

            def queries_low(n):
                dve.wait_ge(q_ready, n + 1)
                nc.vector.tensor_tensor(q_sb[:, 0, :, :], pt_bank[1][:, 0:DT * S].rearrange("p (m s) -> p m s", m=DT),
                                        bq_sb[:].rearrange("p (m a) -> p m a", a=1).broadcast_to([P, DT, S]),
                                        ALU.add).then_inc(q_scaled, 1)
                dve.wait_ge(q_scaled, 2 * n + 1)
                nc.vector.tensor_scalar(q_sb[:, 1, :, :], q_sb[:, 0, :, :], SCALE, None, ALU.mult).then_inc(q_scaled, 1)
                for q in range(HQ):
                    rows = slice(q * HD, (q + 1) * HD)
                    dve.wait_ge(q_hi, HQ * n + q + 1)
                    nc.vector.tensor_tensor(q_pad[1][rows, :, q, :], q_sb[rows, 1, :, :],
                                            q_pad[0][rows, :, q, :].bitcast(F32), ALU.subtract).then_inc(q_lo, 1)

            def score(b, h):
                dve.wait_ge(scores_ready, H * b + h + 1)
                held()
                nc.vector.tensor_tensor_reduce(
                    out=probs[:, h % SCORE_BUFS, 0:T].rearrange("s (a t) -> s a t", a=2),
                    in0=score_pair[h % 2][:, :, 0:HALF], in1=mask_sb[:].rearrange("s (a t) -> s a t", a=2),
                    scale=-1.0, scalar=BIG, op0=ALU.add, op1=ALU.min,
                    accum_out=neg_max[:, h:h + 1]).then_inc(scored, 1)

            def keep_pair(b, pair):
                dve.wait_ge(pair_part, HP * b + pair + 1)
                src = o_bank[pair % 2][0:2 * HD, 0:4 * S].rearrange("p (a x s) -> p a x s", a=2, x=2)
                nc.vector.tensor_tensor(o_heads[:, 2 * pair:2 * pair + 2, :], src[:, :, 0, :], pair_low[:],
                                        ALU.add).then_inc(pair_kept, 1)

            def probs_low(b, h):
                for g in range(2):
                    dve.wait_ge(pt_hi, 2 * H * b + 2 * h + g + 1)
                    nc.vector.tensor_tensor(p_t[:, h % 2, 3 * g:3 * g + 3, 1, :],
                                            pt_bank[g][0:TT, 0:3 * S].rearrange("t (i s) -> t i s", i=3),
                                            p_t[:, h % 2, 3 * g:3 * g + 3, 0, :].bitcast(F32),
                                            ALU.subtract).then_inc(pt_lo, 1)

            def heads(b, n):
                for s in range(1, H + 4):
                    if s < H:
                        score(b, s)
                    if 2 <= s < H + 2:
                        probs_low(b, s - 2)
                    if s >= 5 and s % 2 == 1:
                        keep_pair(b, (s - 5) // 2)
                    if n is not None and s >= H:
                        ctx_low(n, s - H)

            def combine_o(b):
                for g in range(2):
                    dve.wait_ge(o_part, 2 * b + g + 1)
                    at = slice(g * 256, (g + 1) * 256)
                    src = o_bank[g][0:S, :].rearrange("s (h x d) -> s h x d", h=8, x=2)[:, :, 0, :]
                    nc.vector.tensor_tensor(o_sb[:, 1, at].rearrange("s (h d) -> s h d", h=8), src,
                                            o_sb[:, 0, at].rearrange("s (h d) -> s h d", h=8),
                                            ALU.add).then_inc(o_step, 1)
                nc.vector.reciprocal(recip_sum[:], exp_sum[:]).then_inc(o_step, 1)
                dve.wait_ge(o_step, 5 * b + 3)
                nc.vector.tensor_tensor(o_sb[:, 0, :].rearrange("s (h d) -> s h d", h=H),
                                        o_sb[:, 1, :].rearrange("s (h d) -> s h d", h=H),
                                        recip_sum[:].rearrange("s (h a) -> s h a", a=1).broadcast_to([S, H, HD]),
                                        ALU.mult).then_inc(o_step, 1)
                dve.wait_ge(o_step, 5 * b + 4)
                nc.vector.tensor_tensor(o_sb[:, 1, :], o_sb[:, 0, :], bv_sb[:], ALU.add).then_inc(o_step, 1)

            def residual(b):
                dve.wait_ge(y_ready, b + 1)
                nc.vector.tensor_tensor(o_sb[:, 0, :], o_bank[1][0:S, :], bo_sb[:], ALU.add).then_inc(x1_step, 1)
                dve.wait_ge(xres_loaded, 16 * b + 16)
                dve.wait_ge(x1_step, 2 * b + 1)
                nc.vector.scalar_tensor_tensor(x_res[:], o_sb[:, 0, :], gate_x[0:S, 0:1], x_res[:],
                                               ALU.mult, ALU.add).then_inc(x1_step, 1)
                dve.wait_ge(x1_step, 2 * b + 2)

            def route_then(b, k, ins):
                ins.then_inc(route_step, 1)
                dve.wait_ge(route_step, ROUTE_STEPS * b + k)
                if k in HELD_AFTER:
                    held()

            def choose(b):
                dve.wait_ge(logits_ready, b + 1)
                route_then(b, 1, nc.vector.tensor_tensor(logits[:], o_bank[1][0:S, 0:E], gb_sb[:], ALU.add))
                route_then(b, 2, nc.vector.reduce_max(row_max[:], logits[:], AX.X))
                route_then(b, 3, nc.vector.tensor_scalar(shifted[:], logits[:], row_max[:, 0:1], None, ALU.subtract))
                dve.wait_ge(route_exp, b + 1)
                route_then(b, 4, nc.vector.reciprocal(row_sum[:, 1:2], row_sum[:, 0:1]))
                route_then(b, 5, nc.vector.tensor_scalar(gates[:, 1, :], gates[:, 0, :], row_sum[:, 1:2], None, ALU.mult))
                route_then(b, 6, nc.vector.max(top_gate[:], gates[:, 1, :]))
                route_then(b, 7, nc.vector.max_index(top_id[:], top_gate[:], gates[:, 1, :]))
                route_then(b, 8, nc.vector.tensor_copy(top_idf[:], top_id[:, 0:2]))
                for k in range(2):
                    route_then(b, 9 + k, nc.vector.tensor_scalar(chosen[:, k, :], expert_id[:], top_idf[:, k:k + 1],
                                                                 None, ALU.is_equal))
                route_then(b, STEP_EITHER, nc.vector.tensor_tensor(either[:], chosen[:, 0, :], chosen[:, 1, :], ALU.add))

            def place(b):
                k = STEP_EITHER
                route_then(b, k + 1, nc.vector.tensor_scalar(x2[:, :, D + 1], top_gate[:, 0:2], gate_f[0:S, 0:1],
                                                             None, ALU.mult))
                for j in range(2):
                    route_then(b, k + 2 + j, nc.vector.tensor_copy(x2[:, j, D:D + 1].bitcast(U32), token[:]))
                route_then(b, k + 4, nc.vector.tensor_scalar(token[:], token[:], float(S), None, ALU.add))
                dve.wait_ge(counted, b + 1)
                route_then(b, k + 5, nc.vector.tensor_tensor(row_of[:], o_bank[1][0:S, EARLIER:EARLIER + E],
                                                             next_row[0:S, :], ALU.add))
                route_then(b, k + 6, nc.vector.tensor_tensor(next_row[:], o_bank[1][:, IN_ALL:IN_ALL + E],
                                                             next_row[:], ALU.add))
                for j in range(2):
                    route_then(b, k + 7 + j, nc.vector.tensor_tensor(row_pick[:, j, :], row_of[:], chosen[:, j, :], ALU.mult))
                route_then(b, k + 9, nc.vector.reduce_sum(row_f[:], row_pick[:], AX.X))
                route_then(b, k + 10, nc.vector.tensor_copy(pair_row[:], row_f[:]))

            def make_table():
                done = [0]

                def then(ins):
                    done[0] += 1
                    ins.then_inc(table_step, 1)
                    dve.wait_ge(table_step, done[0])

                def across(ap, n):
                    return ap.rearrange("p (o a) -> p o a", o=1).broadcast_to([ap.shape[0], n, ap.shape[1]])

                then(nc.vector.tensor_copy(expert_end[:], next_row[0:1, :]))
                then(nc.vector.tensor_tensor(pairs_of[:], next_row[0:1, :], first_row[0:1, :], ALU.subtract))
                then(nc.vector.tensor_tensor(over[:], pairs_of[:].rearrange("p (e o) -> p e o", o=1).broadcast_to([1, E, MAXB]),
                                             block_rows_below[:], ALU.is_gt))
                then(nc.vector.reduce_sum(blocks_of[:], over[:], AX.X))
                then(nc.vector.tensor_tensor(blocks_to[:], across(blocks_of[:], E), up_to[:], ALU.mult))
                then(nc.vector.reduce_sum(blocks_end[:], blocks_to[:], AX.X))
                then(nc.vector.tensor_tensor(ended[:, 0], across(blocks_end[:], NBLOCKS), block_id[:], ALU.is_le))
                then(nc.vector.reduce_sum(table_f[:, 0, :], ended[:, 0], AX.X))
                then(nc.vector.tensor_scalar(block_expert[:], table_f[:, 0, :], float(E - 1), None, ALU.min))
                then(nc.vector.tensor_scalar(shift[:], blocks_of[:], -float(BLOCK), float(REGION), ALU.mult, ALU.add))
                then(nc.vector.tensor_tensor(ended[:, 1], ended[:, 0], across(shift[:], NBLOCKS), ALU.mult))
                then(nc.vector.reduce_sum(table_f[:, 1, :], ended[:, 1], AX.X))
                then(nc.vector.tensor_tensor(table_f[:, 2, :], table_f[:, 1, :], block_start[:], ALU.add))
                then(nc.vector.tensor_scalar(block_row[:], table_f[:, 2, :], float(SPARE_ROW), None, ALU.min))

            def between(b, n):
                if n is not None:
                    dve.wait_ge(xln_loaded, 16 * n + 16)
                    for i in range(0 if b is None else 4, NT):
                        ctx_low(n, i)
                    ln_stats(0, n, x_ln[:])
                    if b is None:
                        weights_low(1)
                        dve.wait_ge(bk_loaded, 16)
                if b is not None:
                    combine_o(b)
                if n is not None:
                    ln_apply(0, n, x_ln[:], xn[:], xn_ready)
                    for j in range(6):
                        keys_low(n, j)
                if b is not None:
                    residual(b)
                    ln_stats(1, b, x_res[:])
                if n is not None:
                    keys_low(n, 6)
                    keys_low(n, 7)
                if b is not None:
                    dve.wait_ge(rows_scattered, 32 * b)
                    ln_apply(1, b, x_res[:], x2[:, 0, 0:D], x2_ready)
                if n is not None:
                    values_low(n, 0)
                    values_low(n, 1)
                if b is not None:
                    choose(b)
                if n is not None:
                    if b is None:
                        dve.wait_ge(small_loaded, 16 * 5)
                    queries_low(n)
                    values_low(n, 2)
                    values_low(n, 3)
                if b is not None:
                    place(b)
                if n is not None:
                    dve.wait_ge(mask_loaded, 16 * n + 16)
                    score(n, 0)
                    values_low(n, 4)
                    values_low(n, 5)

            def weights_low(k):
                dve.wait_ge(w_hi, k + 1)
                hi, lo = (wk_hl, wv_hl)[k]
                nc.vector.tensor_tensor(lo[:], (wo_sb, wq_sb)[k][:], hi[:].bitcast(F32), ALU.subtract).then_inc(w_lo, 1)

            weights_low(0)
            dve.wait_ge(pads_zero, PADS)
            between(None, 0)
            dve.wait_ge(gates_ready, 2)
            dve.wait_ge(route_consts, ROUTE_CONSTS)
            with dve.Fori(0, B - 1) as b:
                heads(b, b + 1)
                between(b, b + 1)
            heads(B - 1, None)
            between(B - 1, None)
            make_table()


CHUNKS_OF = (DT, HT, HT // 2)
EARLY = 5
AHEAD = [(0, k, 0) for k in range(CHUNKS_OF[0])] + [(1, k, 0) for k in range(EARLY)]
SECOND_REST = [(1, k, 0) for k in range(EARLY, CHUNKS_OF[1])]
THIRD_AND_NEXT = [c for k in range(CHUNKS_OF[2]) for c in ((2, k, 0), (0, k, 1))]
NEXT_SECOND = [(1, k, 1) for k in range(EARLY)]
ROWS_AT_START = (2, 3)
IN_BLOCK = SECOND_REST + THIRD_AND_NEXT + NEXT_SECOND
STAGES = 4
ROWS_BEFORE = len(SECOND_REST) + 6


def experts(nc, sb, sem, banks, ident, filling, expert_end, block_expert, block_row,
            xs_dram, w1, b1, w2, b2, w3, b3, out):
    mm_bank, y_bank, xt_bank = banks[0:4], banks[4:6], banks[6:8]
    chunk_loaded = [sem(f"chunk_loaded_{i}") for i in range(STAGES)]
    chunk_hi = [sem(f"w{i}_hi") for i in (1, 2, 3)]
    chunk_lo = [sem(f"w{i}_lo") for i in (1, 2, 3)]
    bias_loaded = sem("bias_loaded")
    b3_loaded = sem("b3_loaded")
    xs_loaded = sem("xs_loaded")
    xs_transposed = sem("xs_transposed")
    xs_hi = sem("xs_hi")
    xs_lo = sem("xs_lo")
    h1_ready = sem("h1_ready")
    h1_gelu = sem("h1_gelu")
    h1_hi = sem("h1_hi")
    h1_lo = sem("h1_lo")
    h2_ready = sem("h2_ready")
    h2_gelu = sem("h2_gelu")
    h2_hi = sem("h2_hi")
    h2_lo = sem("h2_lo")
    y_ready = sem("ye_ready")
    carried_loaded = sem("carried_loaded")
    carried_step = sem("carried_step")
    y_biased = sem("y_biased")
    y_weighed = sem("y_weighed")
    pool_go = sem("pool_go")
    small_go = sem("small_go")
    first_tail_filled = sem("first_tail_filled")
    tails_filled = sem("tails_filled")
    rows_added = sem("rows_added")
    layer_sems = ((h1_ready, h1_gelu, h1_hi, h1_lo), (h2_ready, h2_gelu, h2_hi, h2_lo))

    mem = ExitStack()
    with mem:
        w_hl = [[sb(mem, f"w{i}_{n}", [P, kt, cols], F32R) for n in ("high", "low")]
                for i, (kt, cols) in enumerate(((DT, HID), (HT, HID), (HT, D)), start=1)]
        stage = sb(mem, "stage", [P, STAGES, HID])
        biases = sb(mem, "biases", [P, 2, 2, HT])
        b3_sb = sb(mem, "b3_sb", [P, D])
        xs_sb = sb(mem, "xs_sb", [P, TPB, ROW])
        next_number = sb(mem, "next_number", [P, TPB], U32)
        next_weight = sb(mem, "next_weight", [P, TPB])
        number = sb(mem, "number", [P, TPB], U32)
        weight = sb(mem, "weight", [P, TPB])
        xs_t = [sb(mem, f"xs_t_{n}", [P, DT, BLOCK], F32R) for n in ("high", "low")]
        h_hl = [[sb(mem, f"h{i}_{n}", [P, HT, BLOCK], F32R) for n in ("high", "low")] for i in (1, 2)]
        gelu = sb(mem, "gelu", [P, 2, BLOCK])
        y_biased_sb = sb(mem, "y_biased_sb", [P, TPB, D])
        y_sb = sb(mem, "y_sb", [P, TPB, D])
        block = mem.enter_context(nc.Block())

        def place_in_ring(i, ahead):
            at = i if ahead else len(AHEAD) + i
            return at % STAGES, at // STAGES

        def before_in_stage(i, ahead):
            if ahead:
                return AHEAD[i - STAGES] if i >= STAGES else None
            if i >= STAGES:
                return IN_BLOCK[i - STAGES]
            which, k, of_next = IN_BLOCK[i - STAGES]
            return which, k, of_next - 1

        def chunk_source(which, k):
            kt = 1 if which < 2 else 2
            return slice(k * kt * P, (k + 1) * kt * P), slice(k * kt, (k + 1) * kt), kt

        def tail_rows(end):
            return xs_dram[bass.ds(end, BLOCK), :].rearrange("(t p) d -> p t d", p=P)

        def as_rows(ap):
            return ap.rearrange("a k n -> (a k) n")

        @block.sync
        def _(sp):
            def expert(n):
                return sp.value_load(block_expert[0:1, n:n + 1] if isinstance(n, int)
                                     else block_expert[0:1, bass.ds(n, 1)], min_val=0, max_val=E - 1)

            def load_chunk(n, e, i, ahead=False):
                which, k, of_next = (AHEAD if ahead else IN_BLOCK)[i]
                stage_no, _ = place_in_ring(i, ahead)
                last = before_in_stage(i, ahead)
                if last is not None:
                    sp.wait_ge(chunk_lo[last[0]], CHUNKS_OF[last[0]] * (n + last[2]) + last[1] + 1)
                rows, _, kt = chunk_source(which, k)
                src = as_rows((w1, w2, w3)[which][bass.ds(e, 1), rows, :]).rearrange("(t p) n -> p t n", p=P)
                dst = stage[:, stage_no, :].rearrange("p (t n) -> p t n", t=kt)
                sp.dma_start(dst, src).then_inc(chunk_loaded[stage_no], 16)

            def first_row_of(n):
                return sp.value_load(block_row[0:1, n:n + 1] if isinstance(n, int)
                                     else block_row[0:1, bass.ds(n, 1)], min_val=0, max_val=SPARE_ROW)

            def load_small(n, e, row):
                if not (isinstance(n, int) and n == 0):
                    sp.wait_ge(h1_gelu, HT * (n - 1) + 1)
                    sp.sem_inc(small_go, 1)
                    sp.wait_ge(xs_transposed, TPB * n)
                    sp.wait_ge(carried_loaded, 2 * n)
                    sp.wait_ge(tails_filled, 16 * E)
                src = xs_dram[bass.ds(row, BLOCK), :].rearrange("(t p) d -> p t d", p=P)
                sp.dma_start(xs_sb[:], src).then_inc(xs_loaded, 16)
                for i, vec in enumerate((b1, b2)):
                    sp.dma_start(biases_of(n)[:, i, :],
                                 vec[bass.ds(e, 1), :, :].rearrange("a p t -> (a p) t")).then_inc(bias_loaded, 16)

            def biases_of(n):
                return biases[:, n % 2] if isinstance(n, int) else biases[:, bass.ds(n % 2, 1)].rearrange("p a i t -> p (a i) t")

            def load_b3(n, e):
                if not (isinstance(n, int) and n == 0):
                    sp.wait_ge(y_biased, TPB * n)
                sp.dma_start(b3_sb[:], b3[bass.ds(e, 1), :].broadcast_to([P, D])).then_inc(b3_loaded, 16)

            def loads(n, has_next):
                e_now = expert(n)
                if has_next:
                    e_next, row_next = expert(n + 1), first_row_of(n + 1)
                for i, (_, _, of_next) in enumerate(IN_BLOCK):
                    if i == len(SECOND_REST):
                        load_b3(n, e_now)
                    if i == ROWS_BEFORE and has_next:
                        load_small(n + 1, e_next, row_next)
                    if not of_next:
                        load_chunk(n, e_now, i)
                    elif has_next:
                        load_chunk(n, e_next, i)

            e = expert(0)
            row = first_row_of(0)
            end = sp.value_load(expert_end[0:1, bass.ds(e, 1)], min_val=0, max_val=SPARE_ROW)
            sp.dma_start(tail_rows(end), filling[:]).then_inc(first_tail_filled, 16)
            for i in range(len(AHEAD)):
                if i == ROWS_AT_START[0]:
                    sp.wait_ge(first_tail_filled, 16)
                    load_small(0, e, row)
                load_chunk(0, e, i, ahead=True)
            with sp.Fori(0, NBLOCKS - 1) as n:
                loads(n, True)
            loads(NBLOCKS - 1, False)

        @block.gpsimd
        def _(pool):
            def go():
                pool.sem_inc(pool_go, 1)

            def read_carried(n):
                pool.wait_ge(xs_loaded, 16 * n + 16)
                pool.wait_ge(carried_step, 2 * n)
                go()
                nc.gpsimd.tensor_copy(next_number[:], xs_sb[:, :, D].bitcast(U32)).then_inc(carried_loaded, 1)
                nc.gpsimd.tensor_copy(next_weight[:], xs_sb[:, :, D + 1]).then_inc(carried_loaded, 1)

            def take_carried(n):
                pool.wait_ge(carried_loaded, 2 * n + 2)
                pool.wait_ge(rows_added, 16 * TPB * n)
                go()
                nc.gpsimd.tensor_copy(number[:], next_number[:]).then_inc(carried_step, 1)
                nc.gpsimd.tensor_copy(weight[:], next_weight[:]).then_inc(carried_step, 1)

            def add_rows(n):
                for t in range(TPB):
                    pool.wait_ge(carried_step, 2 * n + 2)
                    pool.wait_ge(y_biased, TPB * n + t + 1)
                    go()
                    nc.gpsimd.tensor_scalar(y_sb[:, t, :], y_biased_sb[:, t, :], weight[:, t:t + 1], None,
                                            ALU.mult).then_inc(y_weighed, 1)
                    pool.wait_ge(y_weighed, TPB * n + t + 1)
                    pool.wait_ge(rows_added, 16 * (TPB * n + t))
                    go()
                    nc.gpsimd.indirect_dma_start(
                        out=out, out_offset=bass.IndirectOffsetOnAxis(ap=number[:, t:t + 1], axis=0),
                        in_=y_sb[:, t, :], in_offset=None, compute_op=ALU.add).then_inc(rows_added, 16)

            read_carried(0)
            take_carried(0)
            pool.wait_ge(chunk_lo[1], CHUNKS_OF[1])
            for e in range(E):
                end = pool.value_load(expert_end[0:1, e:e + 1], min_val=e * REGION, max_val=e * REGION + B * S)
                pool.dma_start(tail_rows(end), filling[:]).then_inc(tails_filled, 16)
            with pool.Fori(0, NBLOCKS - 1) as n:
                read_carried(n + 1)
                add_rows(n)
                take_carried(n + 1)
            add_rows(NBLOCKS - 1)
            pool.wait_ge(rows_added, 16 * TPB * NBLOCKS)

        def hidden_input(layer):
            return (xs_t, DT) if layer == 0 else (h_hl[0], HT)

        @block.tensor
        def _(pe):
            def transpose_rows(n):
                pe.wait_ge(xs_loaded, 16 * n + 16)
                for t in range(TPB):
                    if not (isinstance(n, int) and n == 0):
                        pe.wait_ge(xs_lo, TPB * (n - 1) + t + 1)
                    for c in range(DT):
                        last = nc.tensor.transpose(xt_bank[t][:, c * P:(c + 1) * P],
                                                   xs_sb[:, t, c * P:(c + 1) * P], ident[:])
                    last.then_inc(xs_transposed, 1)

            def hidden(n, layer):
                src, kt = hidden_input(layer)
                w = w_hl[layer]
                ready, g_done, hi_done, lo_done = layer_sems[layer]
                if layer == 0:
                    pe.wait_ge(xs_lo, TPB * n + TPB)
                tiles = [(m, k) for m in range(2) for k in range(kt - 1)] + [(m, kt - 1) for m in range(2)]
                tiles += [(m, k) for m in range(2, HT) for k in range(kt)]
                for m, k in tiles:
                    if k == 0 and m >= 4:
                        pe.wait_ge(g_done, HT * n + m - 3)
                    elif k == 0 and layer == 1:
                        pe.wait_ge(h1_gelu, HT * n + m + 5)
                    if m == 0:
                        pe.wait_ge(chunk_lo[layer], CHUNKS_OF[layer] * n + k + 1)
                        if layer == 1:
                            pe.wait_ge(h1_lo, HT * n + k + 1)
                    for s, (a, c) in enumerate(PRODUCTS):
                        last = nc.tensor.matmul(mm_bank[m % 4][:, 0:BLOCK], w[a][:, k, m * P:(m + 1) * P],
                                                src[c][:, k, :], start=(k == 0 and s == 0),
                                                stop=(k == kt - 1 and s == 2))
                    if k == kt - 1:
                        last.then_inc(ready, 1)

            def output(n):
                for t in range(TPB):
                    if t == 0:
                        pe.wait_ge(y_biased, TPB * n)
                    for k in range(HT):
                        if t == 0:
                            pe.wait_ge(chunk_lo[2], CHUNKS_OF[2] * n + k // 2 + 1)
                            pe.wait_ge(h2_lo, HT * n + k + 1)
                        for s, (a, c) in enumerate(PRODUCTS):
                            last = nc.tensor.matmul(y_bank[t][:], h_hl[1][a][:, k, t * P:(t + 1) * P],
                                                    w_hl[2][c][:, k, :], start=(k == 0 and s == 0),
                                                    stop=(k == HT - 1 and s == 2))
                    last.then_inc(y_ready, 1)

            transpose_rows(0)
            with pe.Fori(0, NBLOCKS - 1) as n:
                hidden(n, 0)
                hidden(n, 1)
                transpose_rows(n + 1)
                output(n)
            hidden(NBLOCKS - 1, 0)
            hidden(NBLOCKS - 1, 1)
            output(NBLOCKS - 1)

        def chunk_places(i, ahead):
            which, k, _ = (AHEAD if ahead else IN_BLOCK)[i]
            _, tiles, kt = chunk_source(which, k)
            src = stage[:, place_in_ring(i, ahead)[0], :].rearrange("p (t n) -> p t n", t=kt)
            return src, w_hl[which][0][:, tiles, :], w_hl[which][1][:, tiles, :]

        def numbers(part):
            return [IN_BLOCK.index(c) for c in part]

        @block.scalar
        def _(act):
            def chunk_high(n, i, ahead=False):
                which, k, of_next = (AHEAD if ahead else IN_BLOCK)[i]
                if k == 0 and not ahead:
                    act.wait_ge((h1_ready, h2_ready, y_ready)[which], (HT, HT, TPB)[which] * (n + of_next))
                stage_no, loads = place_in_ring(i, ahead)
                act.wait_ge(chunk_loaded[stage_no], 16 * (len(IN_BLOCK) // STAGES * n + loads + 1))
                src, hi, _ = chunk_places(i, ahead)
                nc.scalar.activation(hi, src, ACT.Copy).then_inc(chunk_hi[which], 1)

            def rows_high(n):
                for t in range(TPB):
                    act.wait_ge(xs_transposed, TPB * n + t + 1)
                    src = xt_bank[t][:].rearrange("p (c s) -> p c s", c=DT)
                    nc.scalar.activation(xs_t[0][:, :, t * P:(t + 1) * P], src, ACT.Copy).then_inc(xs_hi, 1)

            def bias_of(n, layer, m):
                if isinstance(n, int):
                    return biases[:, n % 2, layer, m:m + 1]
                return biases[:, bass.ds(n % 2, 1), layer, m:m + 1].rearrange("p a b -> p (a b)")

            def gelu_tile(n, layer, m):
                ready, g_done, hi_done, lo_done = layer_sems[layer]
                act.wait_ge(ready, HT * n + m + 1)
                if m >= 2:
                    act.wait_ge(lo_done, HT * n + m - 1)
                elif layer == 1:
                    act.wait_ge(h1_lo, HT * n + HT - 1 + m)
                elif m == 0:
                    act.wait_ge(h2_lo, HT * n)
                nc.scalar.activation(gelu[:, m % 2, :], mm_bank[m % 4][:, 0:BLOCK], ACT.Gelu,
                                     bias=bias_of(n, layer, m)).then_inc(g_done, 1)

            def body(n, has_next):
                act.wait_ge(bias_loaded, 32 * n + 32)
                second_rest = numbers(SECOND_REST)
                for m in range(HT):
                    gelu_tile(n, 0, m)
                    if m % 2 and m // 2 < len(second_rest):
                        chunk_high(n, second_rest[m // 2])
                for m, i in enumerate(numbers(THIRD_AND_NEXT)):
                    gelu_tile(n, 1, m)
                    if m % 2 == 0 or has_next:
                        chunk_high(n, i)
                if has_next:
                    rows_high(n + 1)
                    for i in numbers(NEXT_SECOND):
                        chunk_high(n, i)

            nc.scalar.preload_act_table_set("gelu_and_others")
            for i in range(len(AHEAD)):
                if i == ROWS_AT_START[1]:
                    rows_high(0)
                chunk_high(0, i, ahead=True)
            with act.Fori(0, NBLOCKS - 1) as n:
                body(n, True)
            body(NBLOCKS - 1, False)

        @block.vector
        def _(dve):
            def chunk_low(n, i, ahead=False):
                which, k, of_next = (AHEAD if ahead else IN_BLOCK)[i]
                dve.wait_ge(chunk_hi[which], CHUNKS_OF[which] * (n + of_next) + k + 1)
                src, hi, lo = chunk_places(i, ahead)
                nc.vector.tensor_tensor(lo, src, hi.bitcast(F32), ALU.subtract).then_inc(chunk_lo[which], 1)

            def rows_low(n):
                for t in range(TPB):
                    dve.wait_ge(xs_hi, TPB * n + t + 1)
                    src = xt_bank[t][:].rearrange("p (c s) -> p c s", c=DT)
                    at = slice(t * P, (t + 1) * P)
                    nc.vector.tensor_tensor(xs_t[1][:, :, at], src, xs_t[0][:, :, at].bitcast(F32),
                                            ALU.subtract).then_inc(xs_lo, 1)

            def split_tile(n, layer, m):
                ready, g_done, hi_done, lo_done = layer_sems[layer]
                hi, lo = (h_hl[layer][a][:, m, :] for a in (0, 1))
                dve.wait_ge(g_done, HT * n + m + 1)
                nc.vector.tensor_copy(hi, gelu[:, m % 2, :]).then_inc(hi_done, 1)
                dve.wait_ge(hi_done, HT * n + m + 1)
                nc.vector.tensor_tensor(lo, gelu[:, m % 2, :], hi.bitcast(F32), ALU.subtract).then_inc(lo_done, 1)

            def bias_rows(n):
                dve.wait_ge(b3_loaded, 16 * n + 16)
                for t in range(TPB):
                    dve.wait_ge(y_ready, TPB * n + t + 1)
                    if t == 0:
                        dve.wait_ge(y_weighed, TPB * n)
                    nc.vector.tensor_tensor(y_biased_sb[:, t, :], y_bank[t][:], b3_sb[:], ALU.add).then_inc(y_biased, 1)

            def body(n, has_next):
                second_rest = numbers(SECOND_REST)
                for m in range(HT):
                    split_tile(n, 0, m)
                    if m % 2 and m // 2 < len(second_rest):
                        chunk_low(n, second_rest[m // 2])
                for m, i in enumerate(numbers(THIRD_AND_NEXT)):
                    split_tile(n, 1, m)
                    if m % 2 == 0 or has_next:
                        chunk_low(n, i)
                if has_next:
                    rows_low(n + 1)
                    for i in numbers(NEXT_SECOND):
                        chunk_low(n, i)
                bias_rows(n)

            for i in range(len(AHEAD)):
                if i == ROWS_AT_START[1]:
                    rows_low(0)
                chunk_low(0, i, ahead=True)
            with dve.Fori(0, NBLOCKS - 1) as n:
                body(n, True)
            body(NBLOCKS - 1, False)


_INS = ["x", "ctx_1024", "mask_BxSxS2_ff0", "g_xattn", "g_ffn",
        "L0_xattn_Wq", "L0_xattn_bq", "L0_xattn_Wk", "L0_xattn_bk", "L0_xattn_Wv", "L0_xattn_bv",
        "L0_xattn_Wo", "L0_xattn_bo", "L0_ffn_w1", "L0_ffn_b1", "L0_ffn_w2", "L0_ffn_b2",
        "L0_ffn_w3", "L0_ffn_b3", "L0_ffn_gate_w", "L0_ffn_gate_b"]
_BY_PARTITION = ("L0_xattn_bq", "L0_xattn_bk", "L0_ffn_b1", "L0_ffn_b2")
_TRANSPOSED = ("L0_xattn_Wq", "L0_xattn_Wk", "L0_xattn_Wv", "L0_xattn_Wo")


def kernel(**inputs):
    import concourse.bacc as bacc
    from concourse.bass_utils import run_bass_kernel_spmd

    nc = bacc.Bacc("TRN2", target_bir_lowering=False, num_devices=1)
    arrays, args = {}, []
    for name in _INS:
        a = np.asarray(inputs[name])
        a = np.ascontiguousarray(a.T if name in _TRANSPOSED else a)
        if name in _BY_PARTITION:
            a = np.ascontiguousarray(np.swapaxes(a.reshape(*a.shape[:-1], -1, P), -1, -2))
        arrays[f"in_{name}"] = a
        args.append(nc.dram_tensor(f"in_{name}", a.shape, mybir.dt.from_np(a.dtype), kind="ExternalInput").ap())
    args.append(nc.dram_tensor("out_0", (B * S + BLOCK, D), F32, kind="ExternalOutput").ap())
    build(nc, *args)
    r = run_bass_kernel_spmd(nc, [arrays], core_ids=[0])
    return r.results[0]["out_0"][:B * S].reshape(B, S, D)
```
